# Optimizing a Trainium2 kernel written in Bass

```python
import numpy as np
import jax
import jax.numpy as jnp

def _softmax(x, axis=-1):
    return jax.nn.softmax(x, axis=axis)

def _gelu(x):
    return jax.nn.gelu(x, approximate=True)

def _silu(x):
    return jax.nn.silu(x)

def _sigmoid(x):
    return jax.nn.sigmoid(x)

def _layernorm(x, axis=-1, eps=1e-05):
    m = jnp.mean(x, axis=axis, keepdims=True)
    v = jnp.var(x, axis=axis, keepdims=True)
    return (x - m) / jnp.sqrt(v + eps)

def _scatter_add(tgt, idx, src, axis=0):
    return tgt.at[idx].add(src)

def _segment_sum(src, seg, n):
    return jax.ops.segment_sum(src, seg, n)
kernel_name = 'mk_adaln_ffn_d1_seqx_r8_c01dde'

def setup_inputs(seed: int=0):
    np.random.seed(seed)
    _w = jnp.asarray

    def _rec_inputs():
        import jax
        import jax.numpy as jnp
        _rk = jax.random.key(seed)
        x = -7.109e-05 + 0.9999 * jax.random.normal(jax.random.fold_in(_rk, 1), (32, 32, 256), jnp.float32)
        _lenS = 32 - jax.random.randint(jax.random.fold_in(_rk, 7), (32,), 0, max(1, 32 // 4) + 1, jnp.int32)
        _lenS2 = 32 - jax.random.randint(jax.random.fold_in(_rk, 8), (32,), 0, max(1, 32 // 4) + 1, jnp.int32)
        itok_B_1_198 = jax.random.randint(jax.random.fold_in(_rk, 11), (32,), 1, 199, jnp.int32)
        return (x, itok_B_1_198)
    x, itok_B_1_198 = _rec_inputs()

    def _L0_cond_setup():
        import jax, jax.numpy as jnp
        import numpy as np
        B, C, T = (128, 32, 256)
        S, D = (200, 32)
        key = jax.random.key(seed)
        k1, k2, k3 = jax.random.split(key, 3)
        x = jax.random.normal(k1, (B, C, T), dtype=jnp.float32)
        conditions = jax.random.randint(k2, (B,), 0, S, dtype=jnp.int64)
        weights = jax.random.normal(k3, (S, C, D), dtype=jnp.float32) / jnp.sqrt(jnp.float32(C))
        return {'x': x, 'conditions': conditions, 'weights': weights}
    _L0_cond_all = _L0_cond_setup()
    _L0_cond_in = {k: v for k, v in _L0_cond_all.items() if k in ('weights',)}
    del _L0_cond_all

    def _L0_ffn_setup():
        import jax, jax.numpy as jnp
        import numpy as np

        def _sparsify_2to4(h):
            B, S, I = h.shape
            g = h.reshape(B, S, I // 4, 4)
            a = jnp.abs(g)
            _, idx = jax.lax.top_k(a, 2)
            pos = jnp.arange(4)
            mask = (pos == idx[..., 0:1]) | (pos == idx[..., 1:2])
            return (g * mask.astype(g.dtype)).reshape(B, S, I)
        key = jax.random.key(seed)
        k1, k2, k3, k4 = jax.random.split(key, 4)
        B, S, H, I = (4, 256, 256, 1024)
        x = jax.random.normal(k1, (B, S, H), dtype=jnp.float32)
        w_gate = jax.random.normal(k2, (H, I), dtype=jnp.float32) / np.sqrt(H)
        w_up = jax.random.normal(k3, (H, I), dtype=jnp.float32) / np.sqrt(H)
        w_down = jax.random.normal(k4, (I, H), dtype=jnp.float32) / np.sqrt(I)
        return {'x': x, 'w_gate': w_gate, 'w_up': w_up, 'w_down': w_down}
    _L0_ffn_all = _L0_ffn_setup()
    _L0_ffn_in = {k: v for k, v in _L0_ffn_all.items() if k in ('w_gate', 'w_up', 'w_down')}
    del _L0_ffn_all
    return {'x': x, 'itok_B_1_198': itok_B_1_198, 'L0_cond_weights': _L0_cond_in['weights'], 'L0_ffn_w_gate': _L0_ffn_in['w_gate'], 'L0_ffn_w_up': _L0_ffn_in['w_up'], 'L0_ffn_w_down': _L0_ffn_in['w_down']}

def reference(x, itok_B_1_198, L0_cond_weights, L0_ffn_w_gate, L0_ffn_w_up, L0_ffn_w_down):
    import jax
    import jax.numpy as jnp

    def _L0_cond_ref(x, conditions, weights):
        import jax, jax.numpy as jnp
        import numpy as np
        B, C, T = (128, 32, 256)
        S, D = (200, 32)
        w = weights[conditions]
        return jnp.einsum('bct,bcd->bdt', x, w)

    def _L0_ffn_ref(x, w_gate, w_up, w_down):
        import jax, jax.numpy as jnp
        import numpy as np

        def _sparsify_2to4(h):
            B, S, I = h.shape
            g = h.reshape(B, S, I // 4, 4)
            a = jnp.abs(g)
            _, idx = jax.lax.top_k(a, 2)
            pos = jnp.arange(4)
            mask = (pos == idx[..., 0:1]) | (pos == idx[..., 1:2])
            return (g * mask.astype(g.dtype)).reshape(B, S, I)
        h = jax.nn.silu(jnp.einsum('bsh,hi->bsi', x, w_gate)) * jnp.einsum('bsh,hi->bsi', x, w_up)
        h_sparse = _sparsify_2to4(h)
        return jnp.einsum('bsi,ih->bsh', h_sparse, w_down)
    x = x + _L0_ffn_ref(_L0_cond_ref(x, itok_B_1_198, L0_cond_weights), L0_ffn_w_gate, L0_ffn_w_up, L0_ffn_w_down)
    return x

_drawn_inputs = setup_inputs


def setup_inputs(seed=0):
    import zlib

    import numpy as np

    out = dict(_drawn_inputs(seed))
    spreads = {}
    factors = {}
    for name, (base, spread) in spreads.items():
        noise = np.random.default_rng([zlib.crc32(name.encode()), seed]).standard_normal(out[name].shape)
        drawn = base * np.exp(spread * noise) if base else spread * noise
        out[name] = jnp.asarray(drawn.astype(out[name].dtype))
    for name, factor in factors.items():
        out[name] = (out[name] * factor).astype(out[name].dtype)
    return out
```

```python
import concourse.bass as bass
from concourse import mybir
from contextlib import ExitStack


def adaln_ffn(nc: bass.Bass, x: bass.AP, cond: bass.AP, cond_w: bass.AP, w_gate: bass.AP,
              w_up: bass.AP, w_down: bass.AP, out: bass.AP):
    f32 = mybir.dt.float32
    f32r = mybir.dt.float32r
    bf16 = mybir.dt.bfloat16
    i32 = mybir.dt.int32
    ALU = mybir.AluOpType
    ACT = mybir.ActivationFunctionType

    P = 128
    B, C, T = x.shape
    S, _, D = cond_w.shape
    I = w_gate.shape[1]
    NB = P // C
    NG = B // NB
    KT = T // P
    M = 4
    NQ = I // (M * P)
    NH = 2
    TH = B * D // NH
    GH = NG // NH
    UNITS = [(half, q) for half in range(NH) for q in range(NQ)]
    PAIRS = len(UNITS) * M
    RING = 4
    HI, LO = 0, 1

    x_v = x.rearrange("(g b) c t -> (b c) g t", b=NB)
    out_v = out.rearrange("(g b) c t -> (b c) g t", b=NB)
    gate_v = w_gate.rearrange("(k p) (q n) -> p k q n", p=P, q=NQ)
    up_v = w_up.rearrange("(k p) (q n) -> p k q n", p=P, q=NQ)
    down_v = w_down.rearrange("(q p j) h -> p q (j h)", q=NQ, j=M)
    table_v = cond_w.rearrange("s c d -> (s c) d")

    ctx = ExitStack()
    with ctx:
        def sb(name, shape, dt):
            return ctx.enter_context(nc.sbuf_tensor(name, shape, dt))

        def sem(name):
            return ctx.enter_context(nc.semaphore(name))

        x_sb = sb("x_sb", [P, NG, T], f32)
        cond_sb = sb("cond_sb", [P, B], i32)
        chan = sb("chan", [P, 1], f32)
        index = sb("index", [P, NG], i32)
        mix = sb("mix", [P, NG, D], f32)
        mix_diag = sb("mix_diag", [P, NG, NB, D], f32)
        raw_w = [sb("gate_raw", [P, NQ, KT, M * P], f32), sb("up_raw", [P, NQ, KT, M * P], f32)]
        down_raw = sb("down_raw", [P, NQ, M * T], f32)
        w_hl = [sb("gate_hl", [P, 2, NQ, KT, M, P], f32r), sb("up_hl", [P, 2, NQ, KT, M, P], f32r)]
        down_hl = sb("down_hl", [P, NQ, M, 2, T], f32r)
        y_hl = sb("y_hl", [P, 2, NH, KT, TH], f32r)
        silu = sb("silu", [P, 2, TH], f32)
        h = sb("h", [P, 2, M, TH], f32)
        a = sb("a", [P, M, TH], f32)
        wins = sb("wins", [P, 3, 2, TH], bf16)
        sums = sb("sums", [P, 2, 2, TH], bf16)
        count = sb("count", [P, 2, 2, TH], bf16)
        h_hl = sb("h_hl", [P, len(UNITS), 2, M, TH], f32r)

        bank = [ctx.enter_context(nc.psum_tensor(f"bank{i}", [P, TH], f32)) for i in range(2 * RING)]

        cond_in = sem("cond_in")
        x_in = [sem(f"x_in{i}") for i in range(NH)]
        w_in = [[sem(f"gate_in{q}") for q in range(NQ)], [sem(f"up_in{q}") for q in range(NQ)]]
        down_in = sem("down_in")
        chan_done = sem("chan_done")
        index_done = sem("index_done")
        mix_in = [sem(f"mix_in{g}") for g in range(NG)]
        zero_done = sem("zero_done")
        diag_done = sem("diag_done")
        mixed = sem("mixed")
        y_hi = sem("y_hi")
        y_lo = sem("y_lo")
        w_hi = sem("w_hi")
        w_lo = [sem(f"w_lo{q}") for q in range(NQ)]
        down_hi = sem("down_hi")
        down_lo = sem("down_lo")
        pair_done = sem("pair_done")
        silu_done = sem("silu_done")
        h_done = sem("h_done")
        abs_done = sem("abs_done")
        chain = sem("chain")
        masked = sem("masked")
        h_hi = sem("h_hi")
        h_lo = sem("h_lo")
        down_done = sem("down_done")
        out_done = sem("out_done")
        stored = sem("stored")

        block = ctx.enter_context(nc.Block())

        def gate_bank(n):
            return bank[2 * (n % RING)]

        def up_bank(n):
            return bank[2 * (n % RING) + 1]

        def y_bank(half, k):
            return bank[2 * (RING - 1) + k]

        def down_bank(g):
            return bank[g % (2 * RING)]

        W_ORDER = [(q, w) for q in range(NQ) for w in range(2)]

        @block.sync
        def _(sp):
            sp.dma_start(x_sb[:, 0:GH, :], x_v[:, 0:GH, :]).then_inc(x_in[0], 16)
            sp.dma_start(raw_w[1][:, 0], up_v[:, :, 0, :]).then_inc(w_in[1][0], 16)
            sp.dma_start(raw_w[0][:, 1], gate_v[:, :, 1, :]).then_inc(w_in[0][1], 16)
            sp.dma_start(x_sb[:, GH:NG, :], x_v[:, GH:NG, :]).then_inc(x_in[1], 16)
            sp.dma_start(down_raw[:], down_v).then_inc(down_in, 16)
            for g in range(NG):
                sp.wait_ge(out_done, g + 1)
                sp.dma_start(out_v[:, g, :], x_sb[:, g, :]).then_inc(stored, 16)
            sp.wait_ge(stored, 16 * NG)

        @block.gpsimd
        def _(pool):
            pool.iota(chan[:], pattern=[[0, 1]], base=0, channel_multiplier=1,
                      allow_small_or_imprecise_dtypes=True).then_inc(chan_done, 1)
            nc.gpsimd.memset(mix_diag[:], 0.0).then_inc(zero_done, 1)
            pool.wait_ge(index_done, 1)
            for g in range(NG):
                nc.gpsimd.indirect_dma_start(
                    out=mix[:, g, :], out_offset=None, in_=table_v,
                    in_offset=bass.IndirectOffsetOnAxis(ap=index[:, g:g + 1], axis=0),
                ).then_inc(mix_in[g], 16)
            for n, (q, w) in enumerate(W_ORDER):
                if q == 0:
                    continue
                pool.wait_ge(w_in[w][q], 16)
                pool.wait_ge(w_hi, n + 1)
                for k in range(KT):
                    last = nc.gpsimd.tensor_tensor(
                        w_hl[w][:, LO, q, k],
                        raw_w[w][:, q, k].rearrange("p (g j) -> p j g", j=M),
                        w_hl[w][:, HI, q, k].bitcast(f32), ALU.subtract)
                last.then_inc(w_lo[q], 1)
            for q in range(NQ):
                pool.wait_ge(down_hi, q + 1)
                nc.gpsimd.tensor_tensor(
                    down_hl[:, q, :, LO, :], down_raw[:, q].rearrange("p (j h) -> p j h", j=M),
                    down_hl[:, q, :, HI, :].bitcast(f32), ALU.subtract).then_inc(down_lo, 1)

        @block.scalar
        def _(act):
            act.dma_start(cond_sb[:], cond.partition_broadcast(P)).then_inc(cond_in, 16)
            act.dma_start(raw_w[0][:, 0], gate_v[:, :, 0, :]).then_inc(w_in[0][0], 16)
            act.dma_start(raw_w[1][:, 1], up_v[:, :, 1, :]).then_inc(w_in[1][1], 16)

            def high_weights(q, w):
                act.wait_ge(w_in[w][q], 16)
                for k in range(KT):
                    last = nc.scalar.activation(w_hl[w][:, HI, q, k],
                                                raw_w[w][:, q, k].rearrange("p (g j) -> p j g", j=M),
                                                ACT.Copy)
                last.then_inc(w_hi, 1)

            def high_y(half):
                for k in range(KT):
                    act.wait_ge(mixed, KT * half + k + 1)
                    nc.scalar.activation(y_hl[:, HI, half, k], y_bank(half, k)[:], ACT.Copy).then_inc(y_hi, 1)

            def high_down():
                act.wait_ge(down_in, 16)
                for q in range(NQ):
                    nc.scalar.activation(down_hl[:, q, :, HI, :],
                                         down_raw[:, q].rearrange("p (j h) -> p j h", j=M),
                                         ACT.Copy).then_inc(down_hi, 1)

            def gate_silu(n):
                act.wait_ge(pair_done, n + 1)
                if n >= 2:
                    act.wait_ge(h_done, n - 1)
                nc.scalar.activation(silu[:, n % 2], gate_bank(n)[:], ACT.Silu).then_inc(silu_done, 1)

            def absolute(u):
                act.wait_ge(h_done, M * (u + 1))
                if u >= 1:
                    act.wait_ge(masked, u)
                nc.scalar.activation(a[:], h[:, u % 2], ACT.Abs).then_inc(abs_done, 1)

            def high_h(u):
                act.wait_ge(masked, u + 1)
                nc.scalar.activation(h_hl[:, u, HI], h[:, u % 2], ACT.Copy).then_inc(h_hi, 1)

            high_weights(0, 0)
            high_y(0)
            high_weights(0, 1)
            high_weights(1, 0)
            high_weights(1, 1)
            high_y(1)
            for u in range(len(UNITS)):
                for j in range(M):
                    gate_silu(M * u + j)
                    if u >= 1 and j == M - 1:
                        high_h(u - 1)
                absolute(u)
                if u == 0:
                    high_down()
            high_h(len(UNITS) - 1)

        @block.vector
        def _(dve):
            steps = [0]

            def step(instruction):
                steps[0] += 1
                instruction.then_inc(chain, 1)

            def settle():
                dve.wait_ge(chain, steps[0])

            dve.wait_ge(chan_done, 1)
            dve.wait_ge(cond_in, 16)
            cond_v = cond_sb[:].rearrange("p (g b) -> p b g", b=NB)
            for b in range(NB):
                rows = slice(b * C, (b + 1) * C)
                step(nc.vector.tensor_scalar(index[rows, :], cond_v[rows, b, :], float(C), float(-b * C),
                                             ALU.mult, ALU.add))
            settle()
            nc.vector.tensor_scalar(index[:], index[:], chan[:], None, ALU.add).then_inc(index_done, 1)

            def diagonal(half):
                dve.wait_ge(zero_done, 1)
                tiles = slice(half * GH, (half + 1) * GH)
                for g in range(half * GH, (half + 1) * GH):
                    dve.wait_ge(mix_in[g], 16)
                for b in range(NB):
                    rows = slice(b * C, (b + 1) * C)
                    last = nc.vector.tensor_copy(mix_diag[rows, tiles, b, :], mix[rows, tiles, :])
                    last.then_inc(diag_done, 1)

            def low_weights(q, w):
                n = W_ORDER.index((q, w))
                dve.wait_ge(w_in[w][q], 16)
                dve.wait_ge(w_hi, n + 1)
                for k in range(KT):
                    last = nc.vector.tensor_tensor(
                        w_hl[w][:, LO, q, k],
                        raw_w[w][:, q, k].rearrange("p (g j) -> p j g", j=M),
                        w_hl[w][:, HI, q, k].bitcast(f32), ALU.subtract)
                last.then_inc(w_lo[q], 1)

            def low_y(half):
                for k in range(KT):
                    dve.wait_ge(mixed, KT * half + k + 1)
                    dve.wait_ge(y_hi, KT * half + k + 1)
                    nc.vector.tensor_tensor(y_hl[:, LO, half, k], y_bank(half, k)[:],
                                            y_hl[:, HI, half, k].bitcast(f32), ALU.subtract).then_inc(y_lo, 1)

            def product(n):
                u, j = divmod(n, M)
                if j == 0 and u >= 2:
                    dve.wait_ge(h_lo, u - 1)
                dve.wait_ge(silu_done, n + 1)
                nc.vector.tensor_tensor(h[:, u % 2, j], up_bank(n)[:], silu[:, n % 2],
                                        ALU.mult).then_inc(h_done, 1)

            def compare(u):
                dve.wait_ge(abs_done, u + 1)
                if u >= 1:
                    settle()
                step(nc.vector.tensor_tensor(wins[:, 0], a[:, 0:2], a[:, 2:4], ALU.is_ge))
                step(nc.vector.tensor_tensor(wins[:, 1], a[:, 0:2], a[:, 3:1:-1], ALU.is_ge))
                step(nc.vector.tensor_tensor(wins[:, 2], a[:, 0::2], a[:, 1::2], ALU.is_ge))

            def tally(u):
                settle()
                step(nc.vector.tensor_tensor(sums[:, 0], wins[:, 0], wins[:, 1], ALU.add))
                step(nc.vector.tensor_tensor(sums[:, 1], wins[:, 1], wins[:, 0, ::-1], ALU.add))
                settle()
                if u >= 1:
                    dve.wait_ge(masked, u)
                step(nc.vector.tensor_tensor(count[:, 0], sums[:, :, 0], wins[:, 2], ALU.add))
                step(nc.vector.tensor_tensor(count[:, 1], sums[:, :, 1], wins[:, 2], ALU.subtract))

            def mask(u):
                settle()
                hu = h[:, u % 2]
                for j, (cnt, op, bound) in enumerate([(count[:, 0, 0], ALU.is_ge, 2.0),
                                                      (count[:, 1, 0], ALU.is_ge, 1.0),
                                                      (count[:, 1, 1], ALU.is_le, 0.0),
                                                      (count[:, 0, 1], ALU.is_le, 1.0)]):
                    last = nc.vector.scalar_tensor_tensor(hu[:, j], cnt, bound, hu[:, j], op, ALU.mult)
                    if j < M - 1:
                        step(last)
                last.then_inc(masked, 1)

            def low_h(u):
                dve.wait_ge(masked, u + 1)
                dve.wait_ge(h_hi, u + 1)
                nc.vector.tensor_tensor(h_hl[:, u, LO], h[:, u % 2], h_hl[:, u, HI].bitcast(f32),
                                        ALU.subtract).then_inc(h_lo, 1)

            def output(g):
                dve.wait_ge(down_done, g + 1)
                step(nc.vector.tensor_tensor(x_sb[:, g, :], down_bank(g)[:, T:2 * T], x_sb[:, g, :], ALU.add))
                settle()
                nc.vector.tensor_tensor(x_sb[:, g, :], down_bank(g)[:, 0:T], x_sb[:, g, :],
                                        ALU.add).then_inc(out_done, 1)

            diagonal(0)
            low_weights(0, 0)
            low_y(0)
            low_weights(0, 1)
            diagonal(1)
            low_y(1)
            for u in range(len(UNITS) + 1):
                stages = [compare, tally, mask, low_h]
                for j in range(M):
                    if u < len(UNITS):
                        product(M * u + j)
                    if u >= 1:
                        stages[j](u - 1)
            for g in range(NG):
                output(g)

        @block.tensor
        def _(pe):
            def mixing(half):
                pe.wait_ge(x_in[half], 16)
                if half > 0:
                    pe.wait_ge(y_lo, KT * half)
                pe.wait_ge(diag_done, NB * (half + 1))
                for k in range(KT):
                    for i in range(GH):
                        g = half * GH + i
                        last = nc.tensor.matmul(y_bank(half, k)[:, i * P:(i + 1) * P],
                                                x_sb[:, g, k * P:(k + 1) * P],
                                                mix_diag[:, g].rearrange("p b d -> p (b d)"),
                                                start=True, stop=True)
                    last.then_inc(mixed, 1)

            def split_product(dst, stationary, moving):
                terms = [(HI, HI), (HI, LO), (LO, HI)]
                for k in range(KT):
                    for t, (s, m) in enumerate(terms):
                        last = nc.tensor.matmul(dst, stationary(s, k), moving(m, k),
                                                start=(k == 0 and t == 0), stop=(k == KT - 1 and t == 2))
                return last

            def gate_up(n):
                u, j = divmod(n, M)
                half, q = UNITS[u]
                if n >= RING:
                    pe.wait_ge(h_done, n - RING + 1)
                elif n == RING - 1:
                    pe.wait_ge(y_lo, KT * NH)
                if j == 0:
                    pe.wait_ge(y_lo, KT * (half + 1))
                for w, dst in ((0, gate_bank(n)), (1, up_bank(n))):
                    if n == 0 or (j == 0 and half == 0):
                        pe.wait_ge(w_lo[q], w + 1)
                        pe.wait_ge(w_hi, W_ORDER.index((q, w)) + 1)
                    last = split_product(dst[:], lambda s, k: w_hl[w][:, s, q, k, j],
                                         lambda m, k: y_hl[:, m, half, k])
                last.then_inc(pair_done, 1)

            def down(g, qs):
                half, i = divmod(g, GH)
                tokens = slice(i * P, (i + 1) * P)
                for q in qs:
                    u = half * NQ + q
                    pe.wait_ge(h_lo, u + 1)
                    for j in range(M):
                        first, end = q == 0 and j == 0, q == NQ - 1 and j == M - 1
                        nc.tensor.matmul(down_bank(g)[:], h_hl[:, u, HI, j, tokens],
                                         down_hl[:, q, j].rearrange("p s h -> p (s h)"),
                                         start=first, stop=end, skip_group_check=True)
                        last = nc.tensor.matmul(down_bank(g)[:, 0:T], h_hl[:, u, LO, j, tokens],
                                                down_hl[:, q, j, HI], start=False, stop=end,
                                                skip_group_check=True)
                if qs[-1] == NQ - 1:
                    last.then_inc(down_done, 1)

            mixing(0)
            for n in range(PAIRS):
                if n == 2:
                    mixing(1)
                gate_up(n)
            pe.wait_ge(down_lo, NQ)
            for g in range(GH):
                if g == 0:
                    pe.wait_ge(h_done, PAIRS - 2)
                down(g, range(NQ))
            pe.wait_ge(h_done, PAIRS)
            for q in range(NQ):
                for g in range(GH, NG):
                    down(g, [q])


_INS = ["x", "itok_B_1_198", "L0_cond_weights", "L0_ffn_w_gate", "L0_ffn_w_up", "L0_ffn_w_down"]


def kernel(**inputs):
    import numpy as _np
    import concourse.bacc as _bacc
    from concourse import mybir as _mybir
    from concourse.bass_utils import run_bass_kernel_spmd as _run

    nc = _bacc.Bacc("TRN2", target_bir_lowering=False, num_devices=1)
    arrays, args = {}, []
    for name in _INS:
        array = _np.ascontiguousarray(inputs[name])
        arrays[f"in_{name}"] = array
        args.append(nc.dram_tensor(f"in_{name}", array.shape, _mybir.dt.from_np(array.dtype),
                                   kind="ExternalInput").ap())
    out = nc.dram_tensor("out", inputs["x"].shape, _mybir.dt.float32, kind="ExternalOutput").ap()
    adaln_ffn(nc, *args, out)
    result = _run(nc, [arrays], core_ids=[0])
    return result.results[0]["out"]
```

```python
import concourse.bass as bass
from concourse import mybir
from contextlib import ExitStack


def adaln_ffn(nc: bass.Bass, x: bass.AP, cond: bass.AP, cond_w: bass.AP, w_gate: bass.AP,
              w_up: bass.AP, w_down: bass.AP, out: bass.AP):
    f32 = mybir.dt.float32
    f32r = mybir.dt.float32r
    bf16 = mybir.dt.bfloat16
    i32 = mybir.dt.int32
    ALU = mybir.AluOpType
    ACT = mybir.ActivationFunctionType

    P = 128
    B, C, T = x.shape
    S, _, D = cond_w.shape
    I = w_gate.shape[1]
    NB = P // C
    NG = B // NB
    KT = T // P
    M = 4
    NQ = I // (M * P)
    NH = 2
    TH = B * D // NH
    GH = NG // NH
    UNITS = [(half, q) for half in range(NH) for q in range(NQ)]
    PAIRS = len(UNITS) * M
    RING = 3
    BANKS = 8
    WARM_START, WARM_Y = 22, 8
    DOWN_AFTER = {13: [0], 14: [1], 15: [2, 3]}
    LAST = len(UNITS) - 1
    TB = TH // 2
    HI, LO = 0, 1

    x_v = x.rearrange("(g b) c t -> (b c) g t", b=NB)
    out_v = out.rearrange("(g b) c t -> (b c) g t", b=NB)
    gate_v = w_gate.rearrange("(k p) (q n) -> p k q n", p=P, q=NQ)
    up_v = w_up.rearrange("(k p) (q n) -> p k q n", p=P, q=NQ)
    down_v = w_down.rearrange("(q p j) h -> p q (j h)", q=NQ, j=M)
    table_v = cond_w.rearrange("s c d -> s (c d)")

    ctx = ExitStack()
    with ctx:
        def sb(name, shape, dt):
            return ctx.enter_context(nc.sbuf_tensor(name, shape, dt))

        def sem(name):
            return ctx.enter_context(nc.semaphore(name))

        x_sb = sb("x_sb", [P, NG, T], f32)
        cond_sb = sb("cond_sb", [B, 1], i32)
        raw_w = [sb("gate_raw", [P, NQ, KT, M * P], f32), sb("up_raw", [P, NQ, KT, M * P], f32)]
        down_raw = sb("down_raw", [P, NQ, M * T], f32)
        w_hl = [sb("gate_hl", [P, 2, NQ, KT, M, P], f32r), sb("up_hl", [P, 2, NQ, KT, M, P], f32r)]
        down_hl = sb("down_hl", [P, NQ, M, 2, T], f32r)
        y_hl = sb("y_hl", [P, 2, NH, KT, TH], f32r)
        warm = sb("warm", [P, TH], bf16)
        silu = sb("silu", [P, 3, TH], f32)
        h = sb("h", [P, 2, M, TH], f32)
        a = sb("a", [P, 2, M, TH], f32)
        mix_row = h[0:B, 1, 0:2].rearrange("b m t -> b (m t)")
        mix_c = h[0:C, 1, 2:4].rearrange("c m t -> c (m t)").rearrange("c (d b) -> c d b", b=B)
        mix_diag = a[:, 1, 0:2].rearrange("p m t -> p (m t)").rearrange(
            "p (g b d) -> p g b d", g=NG, b=NB)
        wins = sb("wins", [P, 3, 2, TH], bf16)
        sums = sb("sums", [P, 2, 2, TH], bf16)
        count = sb("count", [P, 2, 2, TH], bf16)
        h_hl = sb("h_hl", [P, NQ, 2, M, TH], f32r)

        bank = [ctx.enter_context(nc.psum_tensor(f"bank{i}", [P, TH], f32)) for i in range(BANKS)]

        cond_in = sem("cond_in")
        x_in = [sem(f"x_in{i}") for i in range(NH)]
        w_in = [[sem(f"gate_in{q}") for q in range(NQ)], [sem(f"up_in{q}") for q in range(NQ)]]
        down_in = sem("down_in")
        gather_sent = sem("gather_sent")
        mix_in = sem("mix_in")
        zero_done = sem("zero_done")
        diag_done = sem("diag_done")
        mixed = sem("mixed")
        y_hi = sem("y_hi")
        y_lo = sem("y_lo")
        w_hi = sem("w_hi")
        w_lo = sem("w_lo")
        down_hi = sem("down_hi")
        down_lo = sem("down_lo")
        pair_done = sem("pair_done")
        silu_done = sem("silu_done")
        h_done = sem("h_done")
        abs_done = sem("abs_done")
        chain = sem("chain")
        masked = sem("masked")
        h_hi = sem("h_hi")
        h_lo = sem("h_lo")
        down_done = sem("down_done")
        out_done = sem("out_done")
        warm_zero = sem("warm_zero")
        table_loaded = sem("table_loaded")
        stored = sem("stored")

        block = ctx.enter_context(nc.Block())

        def gate_bank(n):
            return bank[2 * (n % RING)]

        def up_bank(n):
            return bank[2 * (n % RING) + 1]

        def y_bank(k):
            return bank[2 * RING + k]

        def down_bank(g):
            return bank[2 * RING + g] if g < 2 else bank[2 * ((PAIRS - RING + g // 2 - 1) % RING) + g % 2]

        W_ORDER = [(q, w) for q in range(NQ) for w in range(2)]

        @block.sync
        def _(sp):
            sp.dma_start(cond_sb[:], cond.rearrange("(b one) -> b one", one=1)).then_inc(cond_in, 16)
            sp.dma_start(x_sb[:, 0:GH, :], x_v[:, 0:GH, :]).then_inc(x_in[0], 16)
            sp.wait_ge(gather_sent, 1)
            sp.dma_start(raw_w[0][:, 1], gate_v[:, :, 1, :]).then_inc(w_in[0][1], 16)
            sp.dma_start(raw_w[1][:, 1], up_v[:, :, 1, :]).then_inc(w_in[1][1], 16)
            sp.dma_start(x_sb[:, GH:NG, :], x_v[:, GH:NG, :]).then_inc(x_in[1], 16)
            sp.dma_start(down_raw[:], down_v).then_inc(down_in, 16)
            for g in range(NG):
                sp.wait_ge(out_done, g + 1)
                sp.dma_start(out_v[:, g, :], x_sb[:, g, :]).then_inc(stored, 16)
            sp.wait_ge(stored, 16 * NG)

        @block.gpsimd
        def _(pool):
            nc.gpsimd.memset(warm[:], 0.0).then_inc(warm_zero, 1)
            nc.gpsimd.memset(mix_diag, 0.0).then_inc(zero_done, 1)
            pool.wait_ge(cond_in, 16)
            nc.gpsimd.indirect_dma_start(
                out=mix_row, out_offset=None, in_=table_v,
                in_offset=bass.IndirectOffsetOnAxis(ap=cond_sb[:], axis=0),
                engine_sem=gather_sent,
            ).then_inc(mix_in, 16)

        @block.scalar
        def _(act):
            act.dma_start(raw_w[0][:, 0], gate_v[:, :, 0, :]).then_inc(w_in[0][0], 16)
            act.wait_ge(gather_sent, 1)
            act.dma_start(raw_w[1][:, 0], up_v[:, :, 0, :]).then_inc(w_in[1][0], 16)

            def high_weights(q, w):
                act.wait_ge(w_in[w][q], 16)
                for k in range(KT):
                    last = nc.scalar.activation(w_hl[w][:, HI, q, k],
                                                raw_w[w][:, q, k].rearrange("p (g j) -> p j g", j=M),
                                                ACT.Copy)
                last.then_inc(w_hi, 1)

            def high_y(half):
                for k in range(KT):
                    act.wait_ge(mixed, KT * half + k + 1)
                    nc.scalar.activation(y_hl[:, HI, half, k], y_bank(k)[:], ACT.Copy).then_inc(y_hi, 1)

            def high_down():
                act.wait_ge(down_in, 16)
                for q in range(NQ):
                    nc.scalar.activation(down_hl[:, q, :, HI, :],
                                         down_raw[:, q].rearrange("p (j h) -> p j h", j=M),
                                         ACT.Copy).then_inc(down_hi, 1)

            def gate_silu(n):
                act.wait_ge(pair_done, n + 1)
                if n >= 3:
                    act.wait_ge(h_done, n - 2)
                nc.scalar.activation(silu[:, n % 3], gate_bank(n)[:], ACT.Silu).then_inc(silu_done, 1)

            def absolute(n):
                u, j = divmod(n, M)
                act.wait_ge(h_done, n + 1)
                if j == 0 and u >= 2:
                    act.wait_ge(masked, M * (u - 1))
                nc.scalar.activation(a[:, u % 2, j], h[:, u % 2, j], ACT.Abs).then_inc(abs_done, 1)

            def high_h(u):
                for j in range(M):
                    act.wait_ge(masked, M * u + j + 1)
                    nc.scalar.activation(h_hl[:, u, HI, j], h[:, u % 2, j], ACT.Copy).then_inc(h_hi, 1)

            act.wait_ge(warm_zero, 1)
            nc.scalar.activation(silu[:, 0, 0:2], warm[:, 0:2], ACT.Silu).then_inc(table_loaded, 1)
            high_weights(0, 0)
            high_y(0)
            high_weights(0, 1)
            high_weights(1, 0)
            high_weights(1, 1)
            act.wait_ge(table_loaded, 1)
            for n in range(PAIRS):
                u, j = divmod(n, M)
                gate_silu(n)
                if n >= 1:
                    absolute(n - 1)
                if n == 0:
                    high_y(1)
                elif n == 1:
                    high_down()
                if 1 <= u <= NQ and j == M - 1:
                    high_h(u - 1)
            absolute(PAIRS - 1)

        @block.vector
        def _(dve):
            steps = [0]

            def step(instruction):
                steps[0] += 1
                instruction.then_inc(chain, 1)

            def settle():
                dve.wait_ge(chain, steps[0])

            def diagonal():
                dve.wait_ge(mix_in, 16)
                step(nc.vector.transpose(mix_c, mix_row.rearrange("b (c d) -> b d c", c=C)))
                settle()
                dve.wait_ge(zero_done, 1)
                for b in range(NB):
                    last = nc.vector.tensor_copy(mix_diag[b * C:(b + 1) * C, :, b, :],
                                                 mix_c[:, :, b::NB].rearrange("c d g -> c g d"))
                    last.then_inc(diag_done, 1)

            def low_weights(q, w):
                n = W_ORDER.index((q, w))
                dve.wait_ge(w_in[w][q], 16)
                dve.wait_ge(w_hi, n + 1)
                for k in range(KT):
                    last = nc.vector.tensor_tensor(
                        w_hl[w][:, LO, q, k],
                        raw_w[w][:, q, k].rearrange("p (g j) -> p j g", j=M),
                        w_hl[w][:, HI, q, k].bitcast(f32), ALU.subtract)
                last.then_inc(w_lo, 1)

            def low_y(half):
                for k in range(KT):
                    dve.wait_ge(mixed, KT * half + k + 1)
                    dve.wait_ge(y_hi, KT * half + k + 1)
                    nc.vector.tensor_tensor(y_hl[:, LO, half, k], y_bank(k)[:],
                                            y_hl[:, HI, half, k].bitcast(f32), ALU.subtract).then_inc(y_lo, 1)

            def product(n):
                u, j = divmod(n, M)
                if j == 0 and u >= 2:
                    dve.wait_ge(h_lo, M * (u - 1))
                dve.wait_ge(silu_done, n + 1)
                nc.vector.tensor_tensor(h[:, u % 2, j], up_bank(n)[:], silu[:, n % 3],
                                        ALU.mult).then_inc(h_done, 1)

            def compare(u, t):
                dve.wait_ge(abs_done, M * (u + 1))
                if u >= 1:
                    settle()
                au = a[:, u % 2, :, t]
                step(nc.vector.tensor_tensor(wins[:, 0, :, t], au[:, 0:2], au[:, 2:4], ALU.is_ge))
                step(nc.vector.tensor_tensor(wins[:, 1, :, t], au[:, 0:2], au[:, 3:1:-1], ALU.is_ge))
                step(nc.vector.tensor_tensor(wins[:, 2, :, t], au[:, 0::2], au[:, 1::2], ALU.is_ge))

            def tally(u, t):
                done = M * u + (M if t.start else 0)
                settle()
                step(nc.vector.tensor_tensor(sums[:, 0, :, t], wins[:, 0, :, t], wins[:, 1, :, t], ALU.add))
                step(nc.vector.tensor_tensor(sums[:, 1, :, t], wins[:, 1, :, t], wins[:, 0, ::-1, t], ALU.add))
                settle()
                if done:
                    dve.wait_ge(masked, done)
                step(nc.vector.tensor_tensor(count[:, 0, :, t], sums[:, :, 0, t], wins[:, 2, :, t], ALU.add))
                step(nc.vector.tensor_tensor(count[:, 1, :, t], sums[:, :, 1, t], wins[:, 2, :, t], ALU.subtract))

            def mask(u, t):
                settle()
                for j, (which, op, bound) in enumerate([((0, 0), ALU.is_ge, 2.0), ((1, 0), ALU.is_ge, 1.0),
                                                        ((1, 1), ALU.is_le, 0.0), ((0, 1), ALU.is_le, 1.0)]):
                    hj = h[:, u % 2, j, t]
                    nc.vector.scalar_tensor_tensor(hj, count[:, which[0], which[1], t], bound, hj,
                                                   op, ALU.mult).then_inc(masked, 1)

            def low_down(q):
                dve.wait_ge(down_hi, q + 1)
                nc.vector.tensor_tensor(
                    down_hl[:, q, :, LO, :], down_raw[:, q].rearrange("p (j h) -> p j h", j=M),
                    down_hl[:, q, :, HI, :].bitcast(f32), ALU.subtract).then_inc(down_lo, 1)

            def low_h(u, _):
                for j in range(M):
                    dve.wait_ge(masked, M * u + j + 1)
                    dve.wait_ge(h_hi, M * u + j + 1)
                    nc.vector.tensor_tensor(h_hl[:, u, LO, j], h[:, u % 2, j], h_hl[:, u, HI, j].bitcast(f32),
                                            ALU.subtract).then_inc(h_lo, 1)

            def output(g):
                dve.wait_ge(down_done, g + 1)
                if g < GH:
                    step(nc.vector.tensor_tensor(x_sb[:, g, :], down_bank(g)[:, T:2 * T], x_sb[:, g, :],
                                                 ALU.add))
                    settle()
                nc.vector.tensor_tensor(x_sb[:, g, :], down_bank(g)[:, 0:T], x_sb[:, g, :],
                                        ALU.add).then_inc(out_done, 1)

            diagonal()
            low_weights(0, 0)
            low_y(0)
            low_weights(0, 1)
            low_weights(1, 0)
            low_weights(1, 1)
            whole = slice(0, TH)
            for n in range(PAIRS):
                u, j = divmod(n, M)
                product(n)
                if n == 1:
                    low_y(1)
                elif n in (2, 3):
                    low_down(n - 2)
                if u >= 1 and (j < M - 1 or u <= NQ):
                    [compare, tally, mask, low_h][j](u - 1, whole)
            for t in range(0, TH, TB):
                for stage in (compare, tally, mask):
                    stage(LAST, slice(t, t + TB))
            for g in range(NG):
                output(g)

        @block.tensor
        def _(pe):
            def warm_up(times):
                for _ in range(times):
                    nc.tensor.matmul(bank[0][:], warm[:, 0:P], warm[:], start=True, stop=True)

            def mixing(half):
                pe.wait_ge(x_in[half], 16)
                if half > 0:
                    pe.wait_ge(y_lo, KT * half)
                pe.wait_ge(diag_done, NB)
                for k in range(KT):
                    for i in range(GH):
                        g = half * GH + i
                        last = nc.tensor.matmul(y_bank(k)[:, i * P:(i + 1) * P],
                                                x_sb[:, g, k * P:(k + 1) * P],
                                                mix_diag[:, g].rearrange("p b d -> p (b d)"),
                                                start=True, stop=True)
                    last.then_inc(mixed, 1)

            def split_product(n, dst, stationary, moving, half):
                for k in range(KT):
                    if n == 0:
                        pe.wait_ge(y_hi, k + 1)
                    nc.tensor.matmul(dst, stationary(HI, k), moving(HI, k), start=k == 0, stop=False)
                    nc.tensor.matmul(dst, stationary(LO, k), moving(HI, k), start=False, stop=False)
                    if n == 0 or n == 2 * M:
                        pe.wait_ge(y_lo, KT * half + k + 1)
                    last = nc.tensor.matmul(dst, stationary(HI, k), moving(LO, k), start=False, stop=k == KT - 1)
                return last

            def gate_up(n):
                u, j = divmod(n, M)
                half, q = UNITS[u]
                if n >= RING:
                    pe.wait_ge(h_done, n - RING + 1)
                for w, dst in ((0, gate_bank(n)), (1, up_bank(n))):
                    if n == 0 or (j == 0 and half == 0):
                        pe.wait_ge(w_lo, W_ORDER.index((q, w)) + 1)
                        pe.wait_ge(w_hi, W_ORDER.index((q, w)) + 1)
                    last = split_product(n, dst[:], lambda s, k: w_hl[w][:, s, q, k, j],
                                         lambda m, k: y_hl[:, m, half, k], half)
                last.then_inc(pair_done, 1)

            def down(g, qs):
                half, i = divmod(g, GH)
                tokens = slice(i * P, (i + 1) * P)
                for q in qs:
                    u = half * NQ + q
                    if half == 0:
                        pe.wait_ge(h_lo, M * (u + 1))
                    else:
                        pe.wait_ge(masked, M * (u + 1 + (i * P // TB if u == LAST else 0)))
                    for j in range(M):
                        first, end = q == 0 and j == 0, q == NQ - 1 and j == M - 1
                        if half > 0:
                            last = nc.tensor.matmul(down_bank(g)[:, 0:T], h[:, u % 2, j, tokens],
                                                    down_raw[:, q, j * T:(j + 1) * T], start=first, stop=end)
                            continue
                        nc.tensor.matmul(down_bank(g)[:], h_hl[:, u, HI, j, tokens],
                                         down_hl[:, q, j].rearrange("p s h -> p (s h)"),
                                         start=first, stop=end, skip_group_check=True)
                        last = nc.tensor.matmul(down_bank(g)[:, 0:T], h_hl[:, u, LO, j, tokens],
                                                down_hl[:, q, j, HI], start=False, stop=end,
                                                skip_group_check=True)
                if qs[-1] == NQ - 1:
                    last.then_inc(down_done, 1)

            pe.wait_ge(warm_zero, 1)
            warm_up(WARM_START)
            mixing(0)
            warm_up(WARM_Y)
            for n in range(PAIRS):
                if n == 1:
                    mixing(1)
                gate_up(n)
                for g in DOWN_AFTER.get(n, []):
                    if g == 0:
                        pe.wait_ge(down_lo, NQ)
                        pe.wait_ge(y_lo, KT * NH)
                    elif g == 2:
                        pe.wait_ge(h_done, PAIRS - RING + 1)
                    down(g, range(NQ))
            pe.wait_ge(h_done, PAIRS)
            for q in range(NQ):
                for g in range(GH, NG):
                    down(g, [q])


_INS = ["x", "itok_B_1_198", "L0_cond_weights", "L0_ffn_w_gate", "L0_ffn_w_up", "L0_ffn_w_down"]


def kernel(**inputs):
    import numpy as _np
    import concourse.bacc as _bacc
    from concourse import mybir as _mybir
    from concourse.bass_utils import run_bass_kernel_spmd as _run

    nc = _bacc.Bacc("TRN2", target_bir_lowering=False, num_devices=1)
    arrays, args = {}, []
    for name in _INS:
        array = _np.ascontiguousarray(inputs[name])
        arrays[f"in_{name}"] = array
        args.append(nc.dram_tensor(f"in_{name}", array.shape, _mybir.dt.from_np(array.dtype),
                                   kind="ExternalInput").ap())
    out = nc.dram_tensor("out", inputs["x"].shape, _mybir.dt.float32, kind="ExternalOutput").ap()
    adaln_ffn(nc, *args, out)
    result = _run(nc, [arrays], core_ids=[0])
    return result.results[0]["out"]
```

```python
import concourse.bass as bass
from concourse import mybir
from contextlib import ExitStack


def adaln_ffn(nc: bass.Bass, x: bass.AP, cond: bass.AP, cond_w: bass.AP, w_gate: bass.AP,
              w_up: bass.AP, w_down: bass.AP, out: bass.AP):
    f32 = mybir.dt.float32
    f32r = mybir.dt.float32r
    bf16 = mybir.dt.bfloat16
    i32 = mybir.dt.int32
    ALU = mybir.AluOpType
    ACT = mybir.ActivationFunctionType

    P = 128
    B, C, T = x.shape
    S, _, D = cond_w.shape
    I = w_gate.shape[1]
    NB = P // C
    NG = B // NB
    KT = T // P
    M = 4
    NQ = I // (M * P)
    NH = 2
    TH = B * D // NH
    GH = NG // NH
    UNITS = [(half, q) for half in range(NH) for q in range(NQ)]
    PAIRS = len(UNITS) * M
    RING = 3
    WARM_START = 15
    LAST = len(UNITS) - 1
    SPLIT = [0, 2]
    assert UNITS == [(0, 0), (0, 1), (1, 0), (1, 1)]
    DOWN_AFTER = {10: [(0, 0)], 12: [(1, 0)], 15: [(0, 1), (1, 1)]}
    HI, LO = 0, 1

    x_v = x.rearrange("(g b) c t -> (b c) g t", b=NB)
    out_v = out.rearrange("(g b) c t -> (b c) g t", b=NB)
    gate_v = w_gate.rearrange("(k p) (q n) -> p k q n", p=P, q=NQ)
    up_v = w_up.rearrange("(k p) (q n) -> p k q n", p=P, q=NQ)
    down_v = w_down.rearrange("(q p j) h -> p q (j h)", q=NQ, j=M)
    table_v = cond_w.rearrange("s c d -> s (c d)")

    ctx = ExitStack()
    with ctx:
        def sb(name, shape, dt):
            return ctx.enter_context(nc.sbuf_tensor(name, shape, dt))

        def sem(name):
            return ctx.enter_context(nc.semaphore(name))

        x_sb = sb("x_sb", [P, NG, T], f32)
        cond_sb = sb("cond_sb", [B, 1], i32)
        raw_w = [sb("gate_raw", [P, NQ, KT, M * P], f32), sb("up_raw", [P, NQ, KT, M * P], f32)]
        down_raw = sb("down_raw", [P, NQ, M * T], f32)
        w_hl = [sb("gate_hl", [P, 2, NQ, KT, M, P], f32r), sb("up_hl", [P, 2, NQ, KT, M, P], f32r)]
        down_hl = sb("down_hl", [P, 2, M * T], f32r)
        h_hl = sb("h_hl", [P, len(SPLIT), 2, M, TH], f32r)
        y_hl = sb("y_hl", [P, 2, NH, KT, TH], f32r)
        warm = sb("warm", [P, TH], bf16)
        silu = sb("silu", [P, 3, TH], f32)
        h = sb("h", [P, len(UNITS), M, TH], f32)
        a = sb("a", [P, 2, M, TH], f32)
        mix_row = h[0:B, 1, 0:2].rearrange("b m t -> b (m t)")
        mix_c = h[0:C, 1, 2:4].rearrange("c m t -> c (m t)").rearrange("c (d b) -> c d b", b=B)
        mix_diag = a[:, 1, 0:2].rearrange("p m t -> p (m t)").rearrange(
            "p (g b d) -> p g b d", g=NG, b=NB)
        far = sb("far", [P, 4, TH], bf16)
        near = sb("near", [P, 2, TH], bf16)
        sums = sb("sums", [P, M, TH], bf16)
        count = sb("count", [P, M, TH], bf16)

        ring = [ctx.enter_context(nc.psum_tensor(f"bank{i}", [P, TH], f32)) for i in range(2 * RING)]
        y_banks = ctx.enter_context(nc.psum_tensor("y_banks", [P, KT, TH], f32))

        cond_in = sem("cond_in")
        x_in = [sem(f"x_in{i}") for i in range(NH)]
        w_in = [[sem(f"gate_in{q}") for q in range(NQ)], [sem(f"up_in{q}") for q in range(NQ)]]
        first_in = sem("first_in")
        down_in = sem("down_in")
        gather_sent = sem("gather_sent")
        mix_in = sem("mix_in")
        zero_done = sem("zero_done")
        transposed = sem("transposed")
        diag_done = sem("diag_done")
        diag_last_done = sem("diag_last_done")
        mixed = sem("mixed")
        y_hi = sem("y_hi")
        y_lo = sem("y_lo")
        w_hi = sem("w_hi")
        w_lo = sem("w_lo")
        pair_done = sem("pair_done")
        silu_done = sem("silu_done")
        h_done = sem("h_done")
        abs_done = sem("abs_done")
        chain = sem("chain")
        masked = sem("masked")
        down_done = sem("down_done")
        out_done = sem("out_done")
        down_hi = sem("down_hi")
        down_lo = sem("down_lo")
        h_hi = sem("h_hi")
        h_lo = sem("h_lo")
        warm_zero = sem("warm_zero")
        table_loaded = sem("table_loaded")
        stored = sem("stored")

        block = ctx.enter_context(nc.Block())

        def gate_bank(n):
            return ring[2 * (n % RING)]

        def up_bank(n):
            return ring[2 * (n % RING) + 1]

        def down_bank(g):
            return y_banks[:, g, 0:T] if g < 2 else ring[2 * ((PAIRS - RING + g // 2 - 1) % RING) + g % 2][:, 0:T]

        Y_PIECES = [(0, k, k + 1) for k in range(KT)] + [(1, 0, KT)]

        def diagonal_block(b):
            return mix_diag[b * C:(b + 1) * C, :, b, :], mix_c[:, :, b::NB].rearrange("c d g -> c g d")

        PIECES = [(0, w, k, k + 1) for w in range(2) for k in range(KT)] + \
                 [(q, w, 0, KT) for q in range(1, NQ) for w in range(2)]

        def pieces_until(q, w, k):
            return 1 + max(i for i, piece in enumerate(PIECES) if piece[:2] == (q, w) and piece[2] <= k)

        def raw_piece(q, w, k, end):
            return raw_w[w][:, q, k:end].rearrange("p k (g j) -> p k j g", j=M)

        @block.sync
        def _(sp):
            sp.dma_start(cond_sb[:], cond.rearrange("(b one) -> b one", one=1)).then_inc(cond_in, 16)
            sp.wait_ge(gather_sent, 1)
            sp.dma_start(raw_w[1][:, 0], up_v[:, :, 0, :]).then_inc(w_in[1][0], 16)
            sp.dma_start(raw_w[0][:, 1], gate_v[:, :, 1, :]).then_inc(w_in[0][1], 16)
            sp.dma_start(raw_w[1][:, 1], up_v[:, :, 1, :]).then_inc(w_in[1][1], 16)
            sp.dma_start(x_sb[:, GH:NG, :], x_v[:, GH:NG, :]).then_inc(x_in[1], 16)
            sp.dma_start(down_raw[:], down_v).then_inc(down_in, 16)
            for g in range(NG):
                sp.wait_ge(out_done, g + 1)
                sp.dma_start(out_v[:, g, :], x_sb[:, g, :]).then_inc(stored, 16)
            sp.wait_ge(stored, 16 * NG)

        @block.gpsimd
        def _(pool):
            nc.gpsimd.memset(warm[:], 0.0).then_inc(warm_zero, 1)
            nc.gpsimd.memset(mix_diag, 0.0).then_inc(zero_done, 1)
            pool.wait_ge(cond_in, 16)
            nc.gpsimd.indirect_dma_start(
                out=mix_row, out_offset=None, in_=table_v,
                in_offset=bass.IndirectOffsetOnAxis(ap=cond_sb[:], axis=0),
                engine_sem=gather_sent,
            ).then_inc(mix_in, 16)

        @block.scalar
        def _(act):
            act.dma_start(x_sb[:, 0:GH, :], x_v[:, 0:GH, :]).then_inc(x_in[0], 16)
            act.dma_start(raw_w[0][:, 0, 0], gate_v[:, 0, 0, :]).then_inc(first_in, 16)
            act.wait_ge(gather_sent, 1)
            act.dma_start(raw_w[0][:, 0, 1:], gate_v[:, 1:, 0, :]).then_inc(w_in[0][0], 16)

            def high_weights(q, w, k, end):
                act.wait_ge(first_in if (q, w, k) == (0, 0, 0) else w_in[w][q], 16)
                nc.scalar.activation(w_hl[w][:, HI, q, k:end], raw_piece(q, w, k, end), ACT.Copy).then_inc(w_hi, 1)

            def high_y(half, k, end):
                act.wait_ge(mixed, KT * half + end)
                nc.scalar.activation(y_hl[:, HI, half, k:end], y_banks[:, k:end], ACT.Copy).then_inc(y_hi, 1)

            def diagonal():
                act.wait_ge(transposed, 1)
                act.wait_ge(zero_done, 1)
                nc.scalar.activation(*diagonal_block(NB - 1), ACT.Copy).then_inc(diag_last_done, 1)

            def gate_silu(n):
                act.wait_ge(pair_done, n + 1)
                if n >= 3:
                    act.wait_ge(h_done, n - 2)
                nc.scalar.activation(silu[:, n % 3], gate_bank(n)[:], ACT.Silu).then_inc(silu_done, 1)

            def absolute(n):
                u, j = divmod(n, M)
                act.wait_ge(h_done, n + 1)
                if j == 0 and u >= 2:
                    act.wait_ge(masked, M * (u - 1))
                nc.scalar.activation(a[:, u % 2, j], h[:, u, j], ACT.Abs).then_inc(abs_done, 1)

            def high_down():
                act.wait_ge(down_in, 16)
                nc.scalar.activation(down_hl[:, HI], down_raw[:, 0], ACT.Copy).then_inc(down_hi, 1)

            def high_h(u, j):
                act.wait_ge(masked, M * u + j + 2)
                nc.scalar.activation(h_hl[:, SPLIT.index(u), HI, j:j + 2], h[:, u, j:j + 2],
                                     ACT.Copy).then_inc(h_hi, 1)

            act.wait_ge(warm_zero, 1)
            nc.scalar.activation(silu[:, 0, 0:2], warm[:, 0:2], ACT.Silu).then_inc(table_loaded, 1)
            high_weights(*PIECES[0])
            diagonal()
            for piece in PIECES[1:KT]:
                high_weights(*piece)
            for piece in Y_PIECES[:KT]:
                high_y(*piece)
            for piece in PIECES[KT:]:
                high_weights(*piece)
            act.wait_ge(table_loaded, 1)
            for n in range(PAIRS):
                u, j = divmod(n, M)
                gate_silu(n)
                if u == 0:
                    absolute(n)
                elif j >= 1:
                    absolute(n - 1)
                if n == 1:
                    high_y(*Y_PIECES[KT])
                    high_down()
                if u == 1 and j == 2:
                    high_h(0, 0)
                elif u == 1 and j == 3:
                    high_h(0, 2)
                elif u == LAST and j == 3:
                    high_h(LAST - 1, 0)
                if u > 0 and j == M - 1:
                    absolute(n)
            high_h(LAST - 1, 2)

        @block.vector
        def _(dve):
            steps = [0]

            def step(instruction):
                steps[0] += 1
                instruction.then_inc(chain, 1)

            def settle():
                dve.wait_ge(chain, steps[0])

            def diagonal():
                dve.wait_ge(mix_in, 16)
                nc.vector.transpose(mix_c, mix_row.rearrange("b (c d) -> b d c", c=C)).then_inc(transposed, 1)
                dve.wait_ge(transposed, 1)
                dve.wait_ge(zero_done, 1)
                for b in range(NB - 1):
                    nc.vector.tensor_copy(*diagonal_block(b)).then_inc(diag_done, 1)

            def low_weights(i):
                q, w, k, end = PIECES[i]
                dve.wait_ge(first_in if i == 0 else w_in[w][q], 16)
                dve.wait_ge(w_hi, i + 1)
                nc.vector.tensor_tensor(w_hl[w][:, LO, q, k:end], raw_piece(q, w, k, end),
                                        w_hl[w][:, HI, q, k:end].bitcast(f32), ALU.subtract).then_inc(w_lo, 1)

            def low_y(i):
                half, k, end = Y_PIECES[i]
                dve.wait_ge(mixed, KT * half + end)
                dve.wait_ge(y_hi, i + 1)
                nc.vector.tensor_tensor(y_hl[:, LO, half, k:end], y_banks[:, k:end],
                                        y_hl[:, HI, half, k:end].bitcast(f32), ALU.subtract).then_inc(y_lo, 1)

            def product(n):
                u, j = divmod(n, M)
                dve.wait_ge(silu_done, n + 1)
                nc.vector.tensor_tensor(h[:, u, j], up_bank(n)[:], silu[:, n % 3],
                                        ALU.mult).then_inc(h_done, 1)

            def compare_far(u):
                au = a[:, u % 2]
                dve.wait_ge(abs_done, M * (u + 1))
                settle()
                step(nc.vector.tensor_tensor(far.rearrange("p (i j) t -> p i j t", j=2),
                                             au[:, 0:2].unsqueeze(2).broadcast_to([P, 2, 2, TH]),
                                             au[:, 2:4].unsqueeze(1).broadcast_to([P, 2, 2, TH]), ALU.is_ge))

            def compare_near(u):
                au = a[:, u % 2]
                step(nc.vector.tensor_tensor(near[:], au[:, 0::2], au[:, 1::2], ALU.is_ge))

            def compare_early(j):
                if j == 2:
                    dve.wait_ge(abs_done, j)
                    step(nc.vector.tensor_tensor(near[:, 0], a[:, 0, 0], a[:, 0, 1], ALU.is_ge))
                dve.wait_ge(abs_done, j + 1)
                step(nc.vector.tensor_tensor(far[:, j - 2::2], a[:, 0, 0:2],
                                             a[:, 0, j:j + 1].broadcast_to([P, 2, TH]), ALU.is_ge))
                if j == 3:
                    step(nc.vector.tensor_tensor(near[:, 1], a[:, 0, 2], a[:, 0, 3], ALU.is_ge))

            def sum_up(u):
                settle()
                step(nc.vector.tensor_tensor(sums[:, 0:2], far[:, 0::2], far[:, 1::2], ALU.add))
                step(nc.vector.tensor_tensor(sums[:, 2:4], far[:, 0:2], far[:, 2:4], ALU.add))

            def tally(u):
                settle()
                if u >= 1:
                    dve.wait_ge(masked, M * u)
                step(nc.vector.tensor_tensor(count[:, 0::3], sums[:, 0::3], near[:], ALU.add))
                step(nc.vector.tensor_tensor(count[:, 1:3], sums[:, 1:3], near[:], ALU.subtract))
                settle()

            KEEPS = [(ALU.is_ge, 2.0), (ALU.is_ge, 1.0), (ALU.is_le, 0.0), (ALU.is_le, 1.0)]

            def mask(u, members):
                for j in members:
                    op, bound = KEEPS[j]
                    nc.vector.scalar_tensor_tensor(h[:, u, j], count[:, j], bound, h[:, u, j],
                                                   op, ALU.mult).then_inc(masked, 1)

            def low_down():
                dve.wait_ge(down_hi, 1)
                nc.vector.tensor_tensor(down_hl[:, LO], down_raw[:, 0], down_hl[:, HI].bitcast(f32),
                                        ALU.subtract).then_inc(down_lo, 1)

            def low_h(u, j):
                i = SPLIT.index(u)
                dve.wait_ge(masked, M * u + j + 2)
                dve.wait_ge(h_hi, (M * i + j) // 2 + 1)
                nc.vector.tensor_tensor(h_hl[:, i, LO, j:j + 2], h[:, u, j:j + 2],
                                        h_hl[:, i, HI, j:j + 2].bitcast(f32), ALU.subtract).then_inc(h_lo, 1)

            def output(g):
                dve.wait_ge(down_done, g + 1)
                nc.vector.tensor_tensor(x_sb[:, g, :], down_bank(g), x_sb[:, g, :],
                                        ALU.add).then_inc(out_done, 1)

            diagonal()
            for i in range(KT):
                low_weights(i)
            for i in range(KT):
                low_y(i)
            for i in range(KT, len(PIECES)):
                low_weights(i)
            for n in range(PAIRS):
                u, j = divmod(n, M)
                product(n)
                if u == 0:
                    if j == 1:
                        low_y(KT)
                    elif j == 2:
                        low_down()
                        compare_early(2)
                    elif j == 3:
                        compare_early(3)
                elif u == 1:
                    if j == 0:
                        sum_up(0)
                    elif j == 1:
                        tally(0)
                        mask(0, (0, 1))
                    elif j == 2:
                        mask(0, (2, 3))
                    elif j == 3:
                        low_h(0, 0)
                        low_h(0, 2)
                else:
                    if j == 0:
                        compare_far(u - 1)
                    elif j == 1:
                        compare_near(u - 1)
                        sum_up(u - 1)
                    elif j == 2:
                        tally(u - 1)
                        mask(u - 1, (0, 1))
                    elif j == 3:
                        mask(u - 1, (2, 3))
            low_h(LAST - 1, 0)
            compare_far(LAST)
            low_h(LAST - 1, 2)
            compare_near(LAST)
            sum_up(LAST)
            tally(LAST)
            mask(LAST, range(M))
            for g in range(NG):
                output(g)

        @block.tensor
        def _(pe):
            def warm_up(times):
                for _ in range(times):
                    nc.tensor.matmul(ring[0][:], warm[:, 0:P], warm[:], start=True, stop=True)

            def mixing(half):
                pe.wait_ge(x_in[half], 16)
                if half > 0:
                    pe.wait_ge(y_lo, KT * half)
                pe.wait_ge(diag_done, NB - 1)
                pe.wait_ge(diag_last_done, 1)
                for k in range(KT):
                    for i in range(GH):
                        g = half * GH + i
                        last = nc.tensor.matmul(y_banks[:, k, i * P:(i + 1) * P],
                                                x_sb[:, g, k * P:(k + 1) * P],
                                                mix_diag[:, g].rearrange("p b d -> p (b d)"),
                                                start=True, stop=True)
                    last.then_inc(mixed, 1)

            def split_product(dst, w, q, half, j):
                terms = [(s, m, k) for s, ms in ((HI, (HI, LO)), (LO, (HI,))) for k in range(KT) for m in ms]
                for i, (s, m, k) in enumerate(terms):
                    if half == 0 and j == 0:
                        pe.wait_ge(w_hi if s == HI else w_lo, pieces_until(q, w, k))
                    if q == 0 and j == 0:
                        pe.wait_ge(y_hi if m == HI else y_lo, k + 1 if half == 0 else len(Y_PIECES))
                    last = nc.tensor.matmul(dst, w_hl[w][:, s, q, k, j], y_hl[:, m, half, k],
                                            start=i == 0, stop=i == len(terms) - 1)
                return last

            def first_gates():
                terms = [(s, m, k) for k in range(KT) for s, m in ((HI, HI), (LO, HI), (HI, LO))]
                for i, (s, m, k) in enumerate(terms):
                    pe.wait_ge(w_hi if s == HI else w_lo, pieces_until(0, 0, k))
                    pe.wait_ge(y_hi if m == HI else y_lo, k + 1)
                    for n in (0, 1):
                        nc.tensor.matmul(gate_bank(n)[:], w_hl[0][:, s, 0, k, n], y_hl[:, m, 0, k],
                                         start=i == 0, stop=i == len(terms) - 1)

            def gate_up(n):
                u, j = divmod(n, M)
                half, q = UNITS[u]
                if n >= RING:
                    pe.wait_ge(h_done, n - RING + 1)
                for w, dst in ((0, gate_bank(n)), (1, up_bank(n))):
                    if w == 0 and n < 2:
                        continue
                    last = split_product(dst[:], w, q, half, j)
                last.then_inc(pair_done, 1)

            def down(g, q, members=range(M)):
                half, i = divmod(g, GH)
                u = half * NQ + q
                tokens = slice(i * P, (i + 1) * P)
                if u in SPLIT:
                    pe.wait_ge(h_lo, M // 2 * (SPLIT.index(u) + 1))
                else:
                    pe.wait_ge(masked, M * u + members[-1] + 1)
                for j in members:
                    cols = slice(j * T, (j + 1) * T)
                    first, end = q == 0 and j == 0, q == NQ - 1 and j == M - 1
                    if u in SPLIT:
                        hs = h_hl[:, SPLIT.index(u)]
                        for i_term, (m, s) in enumerate(((HI, HI), (HI, LO), (LO, HI))):
                            last = nc.tensor.matmul(down_bank(g), hs[:, m, j, tokens], down_hl[:, s, cols],
                                                    start=first and i_term == 0, stop=False)
                    else:
                        last = nc.tensor.matmul(down_bank(g), h[:, u, j, tokens], down_raw[:, q, cols],
                                                start=first, stop=end)
                if end:
                    last.then_inc(down_done, 1)

            pe.wait_ge(warm_zero, 1)
            warm_up(WARM_START)
            mixing(0)
            first_gates()
            for n in range(PAIRS):
                if n == 2:
                    mixing(1)
                gate_up(n)
                for g, q in DOWN_AFTER.get(n, []):
                    pe.wait_ge(down_in, 16)
                    pe.wait_ge(down_lo, 1)
                    pe.wait_ge(y_lo, len(Y_PIECES))
                    down(g, q)
            for g in (2, 3):
                pe.wait_ge(h_done, PAIRS - RING + 1)
                for q in range(NQ):
                    down(g, q)
            for g in range(GH, NG):
                pe.wait_ge(h_done, PAIRS - RING + g // 2)
                down(g, 0)
            for members in ((0,), (1,)):
                for g in range(GH, NG):
                    down(g, NQ - 1, members)
            for g in range(GH, NG):
                down(g, NQ - 1, (2, 3))


_INS = ["x", "itok_B_1_198", "L0_cond_weights", "L0_ffn_w_gate", "L0_ffn_w_up", "L0_ffn_w_down"]


def kernel(**inputs):
    import numpy as _np
    import concourse.bacc as _bacc
    from concourse import mybir as _mybir
    from concourse.bass_utils import run_bass_kernel_spmd as _run

    nc = _bacc.Bacc("TRN2", target_bir_lowering=False, num_devices=1)
    arrays, args = {}, []
    for name in _INS:
        array = _np.ascontiguousarray(inputs[name])
        arrays[f"in_{name}"] = array
        args.append(nc.dram_tensor(f"in_{name}", array.shape, _mybir.dt.from_np(array.dtype),
                                   kind="ExternalInput").ap())
    out = nc.dram_tensor("out", inputs["x"].shape, _mybir.dt.float32, kind="ExternalOutput").ap()
    adaln_ffn(nc, *args, out)
    result = _run(nc, [arrays], core_ids=[0])
    return result.results[0]["out"]
```
